# Optimizing a Trainium2 kernel written in Bass

```python
import numpy as np
import jax
import jax.numpy as jnp

def _softmax(x, axis=-1):
    return jax.nn.softmax(x, axis=axis)
def _gelu(x):
    return jax.nn.gelu(x, approximate=True)
def _silu(x):
    return jax.nn.silu(x)
def _sigmoid(x):
    return jax.nn.sigmoid(x)
def _layernorm(x, axis=-1, eps=1e-5):
    m = jnp.mean(x, axis=axis, keepdims=True)
    v = jnp.var(x, axis=axis, keepdims=True)
    return (x - m) / jnp.sqrt(v + eps)
def _scatter_add(tgt, idx, src, axis=0):
    return tgt.at[idx].add(src)
def _segment_sum(src, seg, n):
    return jax.ops.segment_sum(src, seg, n)

kernel_name = 'mk_conv_preact_d1_conv_nchw64_12e633'

def setup_inputs(seed: int = 0):
    np.random.seed(seed)
    _w = jnp.asarray
    def _rec_inputs():
        import jax
        import jax.numpy as jnp
        _gk = jax.random.key(seed)
        x = -9.26e-05 + 0.9999 * jax.random.normal(jax.random.fold_in(_gk, 1), (16, 64, 192, 192), jnp.float32)
        return x
    x = _rec_inputs()
    def _L0_conv_setup():
        import jax, jax.numpy as jnp
        import numpy as np
        from jax import lax
        ATT = 16
        SK = 3
        LK = 13
        CIN = 64
        RED = 2

        def _forward(x, w1, b1, w2, b2, lk_filter, fusion_w, fusion_b):
            B, C, H, W = x.shape
            F_att, F_idt = (x[:, :ATT], x[:, ATT:])
            pooled = F_att.mean(axis=(2, 3))
            h1 = jax.nn.gelu(pooled @ w1.T + b1, approximate=False)
            k = (h1 @ w2.T + b2).reshape(B, ATT, SK, SK)
            pad = SK // 2
            xp = jnp.pad(F_att, ((0, 0), (0, 0), (pad, pad), (pad, pad)))
            out_dk = jnp.zeros_like(F_att)
            for i in range(SK):
                for j in range(SK):
                    out_dk = out_dk + xp[:, :, i:i + H, j:j + W] * k[:, :, i, j][:, :, None, None]
            lp = LK // 2
            out_lk = lax.conv_general_dilated(F_att, lk_filter, window_strides=(1, 1), padding=((lp, lp), (lp, lp)), dimension_numbers=('NCHW', 'OIHW', 'NCHW'))
            out = jnp.concatenate([out_lk + out_dk, F_idt], axis=1)
            out = jnp.einsum('bchw,oc->bohw', out, fusion_w) + fusion_b[None, :, None, None]
            return out
        key = jax.random.key(seed)
        ks = jax.random.split(key, 8)
        B, C, H, W = (16, CIN, 192, 192)
        hid = ATT // RED
        x = jax.random.normal(ks[0], (B, C, H, W), dtype=jnp.float32)
        w1 = jax.random.normal(ks[1], (hid, ATT), dtype=jnp.float32) * (1.0 / np.sqrt(ATT))
        b1 = jnp.zeros((hid,), dtype=jnp.float32)
        w2 = jax.random.normal(ks[2], (ATT * SK * SK, hid), dtype=jnp.float32) * 0.02
        b2 = jax.random.normal(ks[3], (ATT * SK * SK,), dtype=jnp.float32) * 0.02
        lk_std = np.sqrt(2.0 / (ATT * LK * LK))
        lk_filter = jax.random.normal(ks[4], (ATT, ATT, LK, LK), dtype=jnp.float32) * lk_std
        fusion_w = jax.random.normal(ks[5], (CIN, CIN), dtype=jnp.float32) * (1.0 / np.sqrt(CIN))
        fusion_b = jax.random.normal(ks[6], (CIN,), dtype=jnp.float32) * 0.01
        return {'x': x, 'w1': w1, 'b1': b1, 'w2': w2, 'b2': b2, 'lk_filter': lk_filter, 'fusion_w': fusion_w, 'fusion_b': fusion_b}
    _L0_conv_all = _L0_conv_setup()
    _L0_conv_in = {k: v for k, v in _L0_conv_all.items() if k in ('w1', 'b1', 'w2', 'b2', 'lk_filter', 'fusion_w', 'fusion_b', )}
    del _L0_conv_all

    return {
        "x": x,
        "L0_conv_w1": _L0_conv_in["w1"],
        "L0_conv_b1": _L0_conv_in["b1"],
        "L0_conv_w2": _L0_conv_in["w2"],
        "L0_conv_b2": _L0_conv_in["b2"],
        "L0_conv_lk_filter": _L0_conv_in["lk_filter"],
        "L0_conv_fusion_w": _L0_conv_in["fusion_w"],
        "L0_conv_fusion_b": _L0_conv_in["fusion_b"],
    }

def reference(x, L0_conv_w1, L0_conv_b1, L0_conv_w2, L0_conv_b2, L0_conv_lk_filter, L0_conv_fusion_w, L0_conv_fusion_b):
    import jax
    import jax.numpy as jnp
    def _L0_conv_ref(x, w1, b1, w2, b2, lk_filter, fusion_w, fusion_b):
        import jax, jax.numpy as jnp
        import numpy as np
        from jax import lax
        ATT = 16
        SK = 3
        LK = 13
        CIN = 64
        RED = 2

        def _forward(x, w1, b1, w2, b2, lk_filter, fusion_w, fusion_b):
            B, C, H, W = x.shape
            F_att, F_idt = (x[:, :ATT], x[:, ATT:])
            pooled = F_att.mean(axis=(2, 3))
            h1 = jax.nn.gelu(pooled @ w1.T + b1, approximate=False)
            k = (h1 @ w2.T + b2).reshape(B, ATT, SK, SK)
            pad = SK // 2
            xp = jnp.pad(F_att, ((0, 0), (0, 0), (pad, pad), (pad, pad)))
            out_dk = jnp.zeros_like(F_att)
            for i in range(SK):
                for j in range(SK):
                    out_dk = out_dk + xp[:, :, i:i + H, j:j + W] * k[:, :, i, j][:, :, None, None]
            lp = LK // 2
            out_lk = lax.conv_general_dilated(F_att, lk_filter, window_strides=(1, 1), padding=((lp, lp), (lp, lp)), dimension_numbers=('NCHW', 'OIHW', 'NCHW'))
            out = jnp.concatenate([out_lk + out_dk, F_idt], axis=1)
            out = jnp.einsum('bchw,oc->bohw', out, fusion_w) + fusion_b[None, :, None, None]
            return out
        return _forward(x, w1, b1, w2, b2, lk_filter, fusion_w, fusion_b)

    def _gn(v, G=32, eps=1e-5):
        B_, C_, H_, W_ = v.shape
        g = v.reshape(B_, G, C_ // G, H_, W_)
        m = jnp.mean(g, axis=(2, 3, 4), keepdims=True)
        s = jnp.var(g, axis=(2, 3, 4), keepdims=True)
        return ((g - m) / jnp.sqrt(s + eps)).reshape(v.shape)

    def _ln_c(v, eps=1e-6):
        m = jnp.mean(v, axis=1, keepdims=True)
        s = jnp.var(v, axis=1, keepdims=True)
        return (v - m) / jnp.sqrt(s + eps)

    def _ln_t(v, eps=1e-5):
        m = jnp.mean(v, axis=-1, keepdims=True)
        s = jnp.var(v, axis=-1, keepdims=True)
        return (v - m) / jnp.sqrt(s + eps)

    def _to_tokens(v):
        B_, C_, H_, W_ = v.shape
        return v.reshape(B_, C_, H_ * W_).transpose(0, 2, 1)
    def _from_tokens(t, like):
        B_, C_, H_, W_ = like.shape
        return t.transpose(0, 2, 1).reshape(B_, C_, H_, W_)

    x = x + _L0_conv_ref(_gn(x), L0_conv_w1, L0_conv_b1, L0_conv_w2, L0_conv_b2, L0_conv_lk_filter, L0_conv_fusion_w, L0_conv_fusion_b)
    return x


_drawn_inputs = setup_inputs


def setup_inputs(seed=0):
    import zlib

    import numpy as np

    out = dict(_drawn_inputs(seed))
    spreads = {'L0_conv_b1': (0.0, 0.8)}
    factors = {'L0_conv_w1': 64.0, 'L0_conv_w2': 8.0, 'L0_conv_b2': 2.718, 'L0_conv_fusion_b': 7.488}
    for name, (base, spread) in spreads.items():
        noise = np.random.default_rng([zlib.crc32(name.encode()), seed]).standard_normal(out[name].shape)
        drawn = base * np.exp(spread * noise) if base else spread * noise
        out[name] = jnp.asarray(drawn.astype(out[name].dtype))
    for name, factor in factors.items():
        out[name] = (out[name] * factor).astype(out[name].dtype)
    return out
```

```python
from contextlib import ExitStack

import concourse.bass as bass
from concourse import mybir

F32 = mybir.dt.float32
F16 = mybir.dt.float16
ALU = mybir.AluOpType
ACT = mybir.ActivationFunctionType
AX = mybir.AxisListType

B, C, H, W = 16, 64, 192, 192
ATT = 16
IDT = C - ATT
HID = 8
LK, SK = 13, 3
PH, PW = 4, 2
NQ = H // PH
XB = W // PW
BY, BX = 4, 7
T = 12
P4 = NQ // T
NCOL = P4 * XB
PIX = P4 * 2 * W
HALF = 2 * W
R = 16
ZROWS = NQ + 3
ZS = 64.0
WS = 1024.0
TINY = 1e-30
MID = [(by, bx) for by in (1, 2) for bx in (2, 3, 4)]
REST = [(by, bx) for by in range(BY) for bx in range(BX) if (by, bx) not in MID]
BLOCKS = MID + REST
NM, NB = len(MID), len(BLOCKS)
ORDER = [(1, 3)] + [k for k in BLOCKS if k != (1, 3)]
NPOS = PH * PW
NT = SK * SK
GN_EPS = 1e-5
EDGE = 6
CHAIN = 34

_C = {}
_at = 0
for _name, _n in (("gx", 128), ("ga", 128), ("ca", 128), ("ones", 128), ("fw", 128), ("w1", HID), ("b1", HID),
                  ("w2", NT * HID), ("b2", NT), ("fb", 1), ("delta", ATT), ("rows", 2), ("tap", NM * NPOS * NT)):
    _C[_name] = (_at, _n)
    _at += _n
NCONST = _at


def build(nc, x, wbase, consts, out):
    with ExitStack() as ctx:
        def sb(name, shape, dt=F32):
            return ctx.enter_context(nc.sbuf_tensor(name, shape, dt))

        def ps(name, shape):
            return ctx.enter_context(nc.psum_tensor(name, shape, F32))

        def sem(name):
            return ctx.enter_context(nc.semaphore(name))

        xr = sb("xr", [128, R, PIX])
        f_z = sb("f_z", [128, PIX])
        f_hi = sb("f_hi", [128, PIX], F16)
        f_lo = sb("f_lo", [128, PIX], F16)
        fused = sb("fused", [128, PIX])
        raw = sb("raw", [128, 2, EDGE, W])
        z_f = sb("z_f", [128, EDGE, XB])
        z_hi = sb("z_hi", [128, ZROWS, XB], F16)
        z_lo = sb("z_lo", [128, ZROWS, XB], F16)
        w_base = sb("w_base", [128, NB, 128])
        w_mid = sb("w_mid", [128, NM * NPOS, ATT])
        w_hi = sb("w_hi", [128, 2, NB, 128], F16)
        w_lo = sb("w_lo", [128, 2, NB, 128], F16)
        a_hi = sb("a_hi", [128, 2, 128], F16)
        a_lo = sb("a_lo", [128, 2, 128], F16)
        cst = sb("cst", [128, NCONST])
        stats = sb("stats", [128, T * 3, 6])
        st = sb("st", [128, 4])
        vg = sb("vg", [128, 2])
        root = sb("root", [128, 2])
        rstd = sb("rstd", [128, 2])
        newt = sb("newt", [128, 2])
        scl = sb("scl", [128, 2, 2])
        shf = sb("shf", [128, 2, 2])
        pooled = sb("pooled", [128, 1])
        pw1 = sb("pw1", [128, HID])
        hpre = sb("hpre", [128, HID])
        hid = sb("hid", [128, HID])
        kprod = sb("kprod", [128, NT, HID])
        kern = sb("kern", [128, NT])
        kmax = sb("kmax", [128, 1])
        lkmax = sb("lkmax", [128, 1])
        wmax = sb("wmax", [128, 1])
        wsafe = sb("wsafe", [128, 1])
        wscale = sb("wscale", [128, 1])
        vprod = sb("vprod", [128, NM * NPOS, NT])
        vtap = sb("vtap", [128, NM * NPOS])
        frow = sb("frow", [128, 3])
        fmax = sb("fmax", [128, 2])
        avec = sb("avec", [128, 1])
        fscale = sb("fscale", [128, 2])
        unscale = sb("unscale", [128, 2])

        conv = ps("conv", [128, 2, 512])
        fus = ps("fus", [128, P4, 512])
        small = ps("small", [128, 512])

        x_load = [sem(f"x_load{k}") for k in range(4)]
        x_store = sem("x_store")
        att_load = [sem(f"att_load{k}") for k in range(2)]
        const_load = sem("const_load")
        base_load = sem("base_load")
        zeroed = sem("zeroed")
        setup_dve = sem("setup_dve")
        setup_max = sem("setup_max")
        conv_done = sem("conv_done")
        fuse_done = sem("fuse_done")
        fused_ready = sem("fused_ready")
        out_ready = sem("out_ready")
        f_idt = sem("f_idt")
        f_idt_lo = sem("f_idt_lo")
        f_conv = sem("f_conv")
        f_ready = sem("f_ready")
        z_high = sem("z_high")
        z_ready = sem("z_ready")
        setup_chain = sem("setup_chain")
        stat_done = sem("stat_done")
        prep_dve = sem("prep_dve")
        group_mean = sem("group_mean")
        group_stats = sem("group_stats")
        hidden_pre = sem("hidden_pre")
        root_ready = sem("root_ready")
        hid_ready = sem("hid_ready")
        max_ready = sem("max_ready")
        w_high = sem("w_high")
        a_high = sem("a_high")
        w_ready = sem("w_ready")

        apart = sem("apart")

        block = ctx.enter_context(nc.Block())

        def c(name, *dims):
            a, n = _C[name]
            return cst[:, a:a + n]

        x_v = x.rearrange("b c (p k l) w -> b k c p (l w)", k=2, l=2)
        out_v = out.rearrange("b c (p k l) w -> b k c p (l w)", k=2, l=2)
        att_v = x.rearrange("b c (p k l) w -> b k l c p w", k=2, l=2)

        def images(eng, image):
            image(eng, 0, 0, True, False)
            with eng.Fori(0, (B - 2) // 2) as i:
                image(eng, 2 * i + 1, 1, False, False)
                image(eng, 2 * i + 2, 0, False, False)
            image(eng, B - 1, (B - 1) % 2, False, True)

        def wait_apart(eng, waited, count):
            eng.wait_ge(waited, count)
            eng.sem_inc(apart, 1)

        def parts_of_x():
            for k in range(2):
                yield k, slice(48 * k, 48 * k + 48), slice(ATT, C)
                yield k, slice(96 + 16 * k, 112 + 16 * k), slice(0, ATT)

        @block.sync
        def _(sp):
            def load_x(b, t, slot, k4, before=None):
                if before is not None:
                    wait_apart(sp, x_load[k4], before)
                for k, part, ch in parts_of_x():
                    sp.dma_start(xr[part, bass.ds(slot, 1), :].rearrange("c s (p n) -> c (s p) n", p=P4),
                                 x_v[bass.ds(b, 1), k, ch, bass.ds(P4 * t, P4), :].rearrange("b c p n -> (b c) p n")
                                 ).then_inc(x_load[k4], 16)

            def store(b, t, slot, m):
                wait_apart(sp, out_ready, m + 1)
                for k, part, ch in parts_of_x():
                    sp.dma_start(out_v[bass.ds(b, 1), k, ch, bass.ds(P4 * t, P4), :].rearrange("b c p n -> (b c) p n"),
                                 xr[part, bass.ds(slot, 1), :].rearrange("c s (p n) -> c (s p) n", p=P4)
                                 ).then_inc(x_store, 16)
                wait_apart(sp, x_store, 64 * (m + 1))

            for m in range(R):
                if m == T - 2:
                    sp.dma_start(w_base[:, :, :], wbase.rearrange("p (k m) -> p k m", m=128)).then_inc(base_load, 16)
                load_x(m // T, m % T, m % R, m % 4, 64 * (m // 4) if m >= 4 else None)
            steps = B * T
            with sp.Fori(0, B - 2) as b:
                with sp.Fori(0, 2) as g:
                    for u in range(4):
                        m = b * T + g * 4 + u
                        store(b, g * 4 + u, m % R, m)
                        load_x(b + 1, g * 4 + u + 4, m % R, u, 64 * (3 * b + g + 4))
                for u in range(4):
                    m = b * T + 8 + u
                    store(b, 8 + u, m % R, m)
                    load_x(b + 2, u, m % R, u, 64 * (3 * b + 2 + 4))
            b = B - 2
            for t in range(8):
                store(b, t, (b * T + t) % R, b * T + t)
                load_x(b + 1, t + 4, (b * T + t) % R, t % 4, 64 * (3 * b + t // 4 + 4))
            for t in range(8, T):
                store(b, t, (b * T + t) % R, b * T + t)
            with sp.Fori(0, T) as t:
                m = (B - 1) * T + t
                store(B - 1, t, m % R, m)
            sp.wait_ge(x_store, 64 * steps)

        def z_parts(t):
            whole = [(0, 128)]
            if isinstance(t, int) and t == 0:
                return [(0, 1, 0, [(32, 64), (96, 128)]), (1, 5, 1, whole)]
            if isinstance(t, int) and t == T - 1:
                return [(46, 2, 0, whole), (48, 1, 2, [(0, 32), (64, 96)])]
            return [(P4 * t + 2, P4, 0, whole)]

        @block.gpsimd
        def _(pool):
            def load_att(b, t, par, s):
                if s is not None:
                    pool.wait_ge(z_high, s - 1)
                for ix in range(PW):
                    for h in range(2):
                        if isinstance(t, int) and t == 0:
                            p0, n, r0 = 0, 5 + h, 1 - h
                        elif isinstance(t, int) and t == T - 1:
                            p0, n, r0 = 45 + h, 3 - h, 0
                        else:
                            p0, n, r0 = P4 * t + 1 + h, P4, 0
                        at = 64 * ix + 32 * h
                        for l in range(2):
                            pool.dma_start(raw[at + 16 * l:at + 16 * l + 16, par, r0:r0 + n, 0:W - 1],
                                           att_v[bass.ds(b, 1), 1 - h, l, 0:ATT, bass.ds(p0, n), ix:ix + W - 1]
                                           .rearrange("b c p w -> (b c) p w")).then_inc(att_load[par], 16)

            nc.gpsimd.memset(z_hi[:, :, :], 0.0).then_inc(zeroed, 1)
            nc.gpsimd.memset(z_lo[:, :, :], 0.0).then_inc(zeroed, 1)
            load_att(0, 0, 0, None)
            load_att(0, 1, 1, None)
            pool.wait_ge(setup_dve, 1)
            nc.gpsimd.partition_all_reduce(fmax[:, :], frow[:, 0:2], 128, bass.bass_isa.ReduceOp.max).then_inc(setup_max, 1)

            def largest(b):
                wait_apart(pool, prep_dve, CHAIN * b + 20)
                nc.gpsimd.partition_all_reduce(wmax[:, :], kmax[:, :], 128,
                                               bass.bass_isa.ReduceOp.max).then_inc(max_ready, 1)

            def image(eng, b, par, first, last):
                with eng.Fori(1, T // 2 - 1) as j:
                    for u in range(2):
                        load_att(b, 2 * j + u, u, b * T + 2 * j + u)
                for t in (T - 2, T - 1):
                    load_att(b, t, t % 2, b * T + t)
                if not last:
                    for t in (0, 1):
                        load_att(b + 1, t, t, (b + 1) * T + t)
                    largest(b + 1)

            largest(0)
            images(pool, image)

        @block.scalar
        def _(act):
            act.dma_start(cst[:, :], consts).then_inc(const_load, 16)

            def evacuate(s, par):
                act.wait_ge(fuse_done, s + 1)
                act.wait_ge(out_ready, s)
                nc.scalar.activation(fused[:, :].rearrange("p (b n) -> p b n", b=P4), fus[:, :, 0:HALF], ACT.Identity,
                                     bias=c("fb"), scale=unscale[:, par:par + 1]).then_inc(fused_ready, 1)

            def evacuate_first(par):
                act.wait_ge(fuse_done, 1)
                nc.scalar.activation(fused[:, :].rearrange("p (b n) -> p b n", b=P4), fus[:, :, 0:HALF], ACT.Identity,
                                     bias=c("fb"), scale=unscale[:, par:par + 1]).then_inc(fused_ready, 1)

            def identity_part(s, par, static):
                if not (isinstance(s, int) and s == 0):
                    act.wait_ge(fuse_done, s)
                    act.wait_ge(f_idt_lo, s)
                src = xr[0:96, bass.ds(s % R, 1), :].rearrange("p s n -> p (s n)")
                nc.scalar.activation(f_z[0:96, :], src, ACT.Identity,
                                     bias=shf[0:96, par, 0:1], scale=scl[0:96, par, 0:1])
                nc.scalar.activation(f_hi[0:96, :], src, ACT.Identity,
                                     bias=shf[0:96, par, 0:1], scale=scl[0:96, par, 0:1]).then_inc(f_idt, 1)

            def conv_part(s, u):
                act.wait_ge(conv_done, s + 1)
                for ox in range(PW):
                    for oyl in range(2):
                        j = 2 * ox + oyl
                        dst = f_hi[96:128, :].rearrange("p (a l x o) -> p a l x o", a=P4, l=2, o=PW)[:, :, oyl, :, ox]
                        src = conv[32 * j:32 * j + 32, u, 0:NCOL].rearrange("p (a x) -> p a x", a=P4)
                        last = nc.scalar.activation(dst, src, ACT.Copy, scale=1.0 / (WS * ZS))
                last.then_inc(f_conv, 1)

            def z_piece(t, par, ipar, s):
                act.wait_ge(att_load[par], 128 * ((s - par) // 2 + 1) if isinstance(s, int) else (s - par) * 64 + 128)
                if not (isinstance(s, int) and s == 0):
                    act.wait_ge(z_ready, s)
                for q0, n, r0, parts in z_parts(t):
                    for a, b in parts:
                        src = raw[a:b, par, r0:r0 + n, 0:W:PW]
                        nc.scalar.activation(z_f[a:b, r0:r0 + n, :], src, ACT.Identity,
                                             bias=shf[a:b, ipar, 1:2], scale=scl[a:b, ipar, 1:2])
                        last = nc.scalar.activation(z_hi[a:b, bass.ds(q0 + 1, n), :], src, ACT.Identity,
                                                    bias=shf[a:b, ipar, 1:2], scale=scl[a:b, ipar, 1:2])
                last.then_inc(z_high, 1)

            def prep_root(b):
                act.wait_ge(prep_dve, CHAIN * b + 4)
                nc.scalar.activation(root[:, :], vg[:, :], ACT.Sqrt).then_inc(root_ready, 1)

            def prep_hidden(b):
                act.wait_ge(prep_dve, CHAIN * b + 15)
                nc.scalar.activation(hid[:, :], hpre[:, :], ACT.Gelu).then_inc(hid_ready, 1)

            def prep_weights(b, par):
                act.wait_ge(prep_dve, CHAIN * b + 34)
                nc.scalar.activation(w_hi[:, par, 0:NM, :], w_mid[:, :, :].rearrange("p (k n) m -> p k (n m)", k=NM),
                                     ACT.Copy, scale=wscale[:, 0:1])
                nc.scalar.activation(w_hi[:, par, NM:NB, :], w_base[:, NM:NB, :],
                                     ACT.Copy, scale=wscale[:, 0:1]).then_inc(w_high, 1)
                nc.scalar.activation(a_hi[:, par, :], c("fw"), ACT.Copy, scale=avec[:, 0:1]).then_inc(a_high, 1)

            def image(eng, b, par, first, last):
                def step(t, u):
                    s = b * T + t
                    if first and isinstance(t, int) and t < 2:
                        pass
                    elif first and isinstance(t, int) and t == 2:
                        evacuate_first(0)
                    else:
                        old = 1 - par if isinstance(t, int) and t < 2 else par
                        evacuate(s - 2, old)
                    if isinstance(t, int) and t == T - 2 and not last:
                        prep_root(b + 1)
                    if not (first and isinstance(t, int) and t == 0):
                        old = 1 - par if isinstance(t, int) and t == 0 else par
                        identity_part(s - 1, old, False)
                        conv_part(s - 1, 1 - u)
                    if isinstance(t, int) and t == T - 1:
                        if not last:
                            prep_weights(b + 1, 1 - par)
                            z_piece(0, 0, 1 - par, (b + 1) * T)
                    else:
                        z_piece(t + 1, 1 - u, par, s + 1)
                    if isinstance(t, int) and t == T - 2 and not last:
                        prep_hidden(b + 1)

                step(0, 0)
                step(1, 1)
                if first:
                    step(2, 0)
                    step(3, 1)
                with eng.Fori(2 if first else 1, T // 2 - 1) as j:
                    step(2 * j, 0)
                    step(2 * j + 1, 1)
                step(T - 2, 0)
                step(T - 1, 1)

            act.wait_ge(zeroed, 2)
            prep_root(0)
            prep_hidden(0)
            prep_weights(0, 0)
            z_piece(0, 0, 0, 0)
            images(act, image)
            last = B * T
            lpar = (B - 1) % 2
            evacuate(last - 2, lpar)
            identity_part(last - 1, lpar, True)
            conv_part(last - 1, (last - 1) % 2)
            evacuate(last - 1, lpar)

        @block.vector
        def _(dve):
            def residual(s):
                dve.wait_ge(fused_ready, s + 1)
                dst = xr[:, bass.ds(s % R, 1), :].rearrange("p s n -> p (s n)")
                nc.vector.tensor_tensor(dst, dst, fused[:, :], ALU.add).then_inc(out_ready, 1)

            def identity_low(s):
                dve.wait_ge(f_idt, s + 1)
                nc.vector.tensor_tensor(f_lo[0:96, :], f_z[0:96, :], f_hi[0:96, :], ALU.subtract).then_inc(f_idt_lo, 1)

            def conv_low(s, u):
                dve.wait_ge(f_conv, s + 1)
                for ox in range(PW):
                    for oyl in range(2):
                        j = 2 * ox + oyl
                        at = [f[96:128, :].rearrange("p (a l x o) -> p a l x o", a=P4, l=2, o=PW)[:, :, oyl, :, ox]
                              for f in (f_lo, f_hi)]
                        src = conv[32 * j:32 * j + 32, u, 0:NCOL].rearrange("p (a x) -> p a x", a=P4)
                        last = nc.vector.scalar_tensor_tensor(out=at[0], in0=src, scalar=1.0 / (WS * ZS), in1=at[1],
                                                              op0=ALU.mult, op1=ALU.subtract)
                last.then_inc(f_ready, 1)

            def z_low(t, s):
                dve.wait_ge(z_high, s + 1)
                for q0, n, r0, parts in z_parts(t):
                    for a, b in parts:
                        rows = bass.ds(q0 + 1, n)
                        last = nc.vector.tensor_tensor(z_lo[a:b, rows, :], z_f[a:b, r0:r0 + n, :], z_hi[a:b, rows, :],
                                                       ALU.subtract)
                last.then_inc(z_ready, 1)

            def statistics(t, s, k4, count):
                dve.wait_ge(x_load[k4], count)
                for n in range(3):
                    nc.vector.bn_stats(stats[:, bass.ds(3 * t + n, 1), :].rearrange("p s n -> p (s n)"),
                                       xr[:, bass.ds(s % R, 1), 512 * n:512 * n + 512].rearrange("p s n -> p (s n)")
                                       ).then_inc(stat_done, 1)

            linked = [0]

            def link_of(b, first):
                linked[0] = first

                def link(ins):
                    ins.then_inc(prep_dve, 1)
                    linked[0] += 1
                    dve.wait_ge(prep_dve, CHAIN * b + linked[0])

                return link

            def prepare_mean(b):
                link = link_of(b, 0)
                wait_apart(dve, stat_done, 3 * T * b + 3 * T)
                link(nc.vector.bn_aggr(st[:, 0:2], stats[:, :, :].rearrange("p s n -> p (s n)")))

            def prepare_variance(b):
                link = link_of(b, 1)
                dve.wait_ge(group_mean, b + 1)
                link(nc.vector.tensor_tensor(st[:, 2:3], st[:, 0:1], small[:, 0:1], ALU.subtract))
                link(nc.vector.scalar_tensor_tensor(out=st[:, 3:4], in0=st[:, 2:3], scalar=st[:, 2:3], in1=st[:, 1:2],
                                                    op0=ALU.mult, op1=ALU.add))
                dve.wait_ge(group_stats, b + 1)
                link(nc.vector.tensor_scalar(vg[:, :], small[:, 7:12:4], GN_EPS, None, ALU.add))

            def prepare_scales(b, par):
                link = link_of(b, 4)
                dve.wait_ge(root_ready, b + 1)
                link(nc.vector.reciprocal(rstd[:, :], root[:, :]))
                link(nc.vector.tensor_tensor(newt[:, :], rstd[:, :], rstd[:, :], ALU.mult))
                link(nc.vector.tensor_tensor(newt[:, :], newt[:, :], vg[:, :], ALU.mult))
                link(nc.vector.tensor_scalar(newt[:, :], newt[:, :], -0.5, 1.5, ALU.mult, ALU.add))
                link(nc.vector.tensor_tensor(rstd[:, :], rstd[:, :], newt[:, :], ALU.mult))
                link(nc.vector.tensor_scalar(scl[:, par, :], rstd[:, :], ZS, None, ALU.mult))
                link(nc.vector.scalar_tensor_tensor(out=shf[:, par, :], in0=small[:, 4:9:4], scalar=-1.0, in1=scl[:, par, :],
                                                    op0=ALU.mult, op1=ALU.mult))
                link(nc.vector.tensor_tensor(pooled[:, :], small[:, 14:15], rstd[:, 1:2], ALU.mult))
                link(nc.vector.tensor_scalar(pw1[:, :], c("w1"), pooled[:, 0:1], None, ALU.mult))

            def prepare_weights(b, par):
                link = link_of(b, 13)
                dve.wait_ge(hidden_pre, b + 1)
                link(nc.vector.tensor_copy(hpre[:, :], small[:, 16:16 + HID]))
                link(nc.vector.tensor_tensor(hpre[:, :], hpre[:, :], c("b1"), ALU.add))
                dve.wait_ge(hid_ready, b + 1)
                link(nc.vector.tensor_tensor(kprod[:, :, :], c("w2").rearrange("p (t j) -> p t j", j=HID),
                                             hid[:, :].rearrange("p (o j) -> p o j", o=1).to_broadcast([128, NT, HID]), ALU.mult))
                link(nc.vector.tensor_reduce(kern[:, :], kprod[:, :, :], AX.X, ALU.add))
                link(nc.vector.tensor_tensor(kern[:, :], kern[:, :], c("b2"), ALU.add))
                link(nc.vector.tensor_reduce(kmax[:, :], kern[:, :], AX.X, ALU.max, apply_absolute_value=True))
                link(nc.vector.tensor_tensor(kmax[:, :], kmax[:, :], lkmax[:, :], ALU.max))
                link(nc.vector.tensor_tensor(vprod[:, :, :], c("tap").rearrange("p (n t) -> p n t", t=NT),
                                             kern[:, :].rearrange("p (o t) -> p o t", o=1).to_broadcast([128, NM * NPOS, NT]), ALU.mult))
                link(nc.vector.tensor_reduce(vtap[:, :], vprod[:, :, :], AX.X, ALU.add))
                link(nc.vector.tensor_tensor(w_mid[:, :, :],
                                             vtap[:, :].rearrange("p (n o) -> p n o", o=1).to_broadcast([128, NM * NPOS, ATT]),
                                             c("delta").rearrange("p (o m) -> p o m", o=1).to_broadcast([128, NM * NPOS, ATT]), ALU.mult))
                link(nc.vector.tensor_tensor(w_mid[:, :, :], w_mid[:, :, :],
                                             w_base[:, 0:NM, :].rearrange("p k (n m) -> p (k n) m", m=ATT), ALU.add))
                dve.wait_ge(max_ready, b + 1)
                link(nc.vector.tensor_scalar(wsafe[:, :], wmax[:, :], TINY, None, ALU.max))
                link(nc.vector.reciprocal(wscale[:, :], wsafe[:, :]))
                link(nc.vector.tensor_scalar(wscale[:, :], wscale[:, :], WS, None, ALU.mult))
                link(nc.vector.tensor_scalar(avec[:, :], wsafe[:, :], c("rows")[:, 0:1], c("rows")[:, 1:2], ALU.mult, ALU.add))
                link(nc.vector.scalar_tensor_tensor(out=fscale[:, 0:1], in0=wsafe[:, :], scalar=fmax[:, 1:2], in1=fmax[:, 0:1],
                                                    op0=ALU.mult, op1=ALU.max))
                link(nc.vector.tensor_scalar(fscale[:, 0:1], fscale[:, 0:1], TINY, None, ALU.max))
                link(nc.vector.reciprocal(fscale[:, 1:2], fscale[:, 0:1]))
                link(nc.vector.tensor_scalar(fscale[:, 1:2], fscale[:, 1:2], WS, None, ALU.mult))
                link(nc.vector.tensor_tensor(avec[:, :], avec[:, :], fscale[:, 1:2], ALU.mult))
                link(nc.vector.tensor_scalar(unscale[:, par:par + 1], fscale[:, 0:1], 1.0 / WS, None, ALU.mult))

            def weights_low(b, par):
                dve.wait_ge(w_high, b + 1)
                nc.vector.scalar_tensor_tensor(out=w_lo[:, par, 0:NM, :].rearrange("p k m -> p (k m)"),
                                               in0=w_mid[:, :, :].rearrange("p n m -> p (n m)"), scalar=wscale[:, 0:1],
                                               in1=w_hi[:, par, 0:NM, :].rearrange("p k m -> p (k m)"),
                                               op0=ALU.mult, op1=ALU.subtract)
                nc.vector.scalar_tensor_tensor(out=w_lo[:, par, NM:NB, :].rearrange("p k m -> p (k m)"),
                                               in0=w_base[:, NM:NB, :].rearrange("p k m -> p (k m)"), scalar=wscale[:, 0:1],
                                               in1=w_hi[:, par, NM:NB, :].rearrange("p k m -> p (k m)"),
                                               op0=ALU.mult, op1=ALU.subtract)
                dve.wait_ge(a_high, b + 1)
                nc.vector.scalar_tensor_tensor(out=a_lo[:, par, :], in0=c("fw"), scalar=avec[:, 0:1], in1=a_hi[:, par, :],
                                               op0=ALU.mult, op1=ALU.subtract).then_inc(w_ready, 1)

            def image(eng, b, par, first, last):
                def step(t, u):
                    s = b * T + t
                    ahead = isinstance(t, int) and t == T - 2 and not last
                    if ahead:
                        prepare_variance(b + 1)
                    if not (first and isinstance(t, int) and t < 2):
                        residual(s - 2)
                    if not (first and isinstance(t, int) and t == 0):
                        identity_low(s - 1)
                        if ahead:
                            prepare_scales(b + 1, 1 - par)
                        conv_low(s - 1, 1 - u)
                    if isinstance(t, int) and t == T - 1:
                        if not last:
                            weights_low(b + 1, 1 - par)
                            z_low(0, (b + 1) * T)
                    else:
                        z_low(t + 1, s + 1)
                    if last:
                        return
                    if isinstance(t, int) and t == 0:
                        for n in range(2):
                            statistics(n, (b + 1) * T + n, n % 4, 64 * 3 * (b + 1) + 64)
                    if ahead:
                        prepare_weights(b + 1, 1 - par)

                def stat(t, k4, group):
                    if not last:
                        statistics(t + 2, (b + 1) * T + t + 2, k4, 64 * 3 * (b + 1) + 64 * (group + 1))

                step(0, 0)
                stat(0, 2, 0)
                step(1, 1)
                stat(1, 3, 0)
                with eng.Fori(0, 2) as j:
                    for u in range(4):
                        step(4 * j + 2 + u, u % 2)
                        stat(4 * j + 2 + u, u, j + 1)
                if not last:
                    prepare_mean(b + 1)
                step(T - 2, 0)
                step(T - 1, 1)

            for t in range(T):
                statistics(t, t, t % 4, 64 * (t // 4 + 1))
            prepare_mean(0)
            dve.wait_ge(const_load, 16)
            dve.wait_ge(base_load, 16)
            nc.vector.tensor_reduce(lkmax[:, :], w_base[:, :, :].rearrange("p k m -> p (k m)"), AX.X, ALU.max,
                                    apply_absolute_value=True).then_inc(setup_chain, 1)
            nc.vector.tensor_reduce(frow[:, 2:3], c("fw"), AX.X, ALU.max, apply_absolute_value=True).then_inc(setup_chain, 1)
            dve.wait_ge(setup_chain, 2)
            nc.vector.tensor_tensor(frow[:, 0:1], frow[:, 2:3], c("rows")[:, 1:2], ALU.mult)
            nc.vector.tensor_tensor(frow[:, 1:2], frow[:, 2:3], c("rows")[:, 0:1], ALU.mult).then_inc(setup_dve, 1)
            prepare_variance(0)
            prepare_scales(0, 0)
            dve.wait_ge(setup_max, 1)
            prepare_weights(0, 0)
            weights_low(0, 0)
            z_low(0, 0)
            images(dve, image)
            last = B * T
            residual(last - 2)
            identity_low(last - 1)
            conv_low(last - 1, (last - 1) % 2)
            residual(last - 1)

        @block.tensor
        def _(pe):
            def group_means(b):
                pe.wait_ge(prep_dve, CHAIN * b + 1)
                nc.tensor.matmul(small[:, 0:1], c("gx"), st[:, 0:1], start=True, stop=True).then_inc(group_mean, 1)

            def group_all(b):
                pe.wait_ge(prep_dve, CHAIN * b + 3)
                for n, m in enumerate(("gx", "ga", "ca")):
                    last = nc.tensor.matmul(small[:, 4 + 4 * n:8 + 4 * n], c(m), st[:, :], start=True, stop=True)
                last.then_inc(group_stats, 1)

            def generator(b):
                pe.wait_ge(prep_dve, CHAIN * b + 13)
                nc.tensor.matmul(small[:, 16:16 + HID], c("ones"), pw1[:, :], start=True, stop=True).then_inc(hidden_pre, 1)

            def convolve(t, par, u, s, between):
                pe.wait_ge(z_ready, s + 1)
                n = 0
                for i, (by, bx) in enumerate(ORDER):
                    if i in between:
                        between[i]()
                    k = BLOCKS.index((by, bx))
                    x0, x1 = max(0, 3 - bx), min(XB, XB + 3 - bx)
                    a0 = 1 if by == 0 and isinstance(t, int) and t == 0 else 0
                    a1 = P4 - 1 if by == BY - 1 and isinstance(t, int) and t == T - 1 else P4
                    dst = conv[:, u, 0:NCOL].rearrange("p (a x) -> p a x", a=P4)[:, a0:a1, x0:x1]
                    rows = bass.ds(P4 * t + by + a0, a1 - a0)
                    for w, z in ((w_hi, z_hi), (w_hi, z_lo), (w_lo, z_hi)):
                        last = nc.tensor.matmul(dst, w[:, par, k, :], z[:, rows, x0 + bx - 3:x1 + bx - 3],
                                                start=(n == 0), stop=(n == 3 * NB - 1))
                        n += 1
                last.then_inc(conv_done, 1)

            def fuse(s, par):
                pe.wait_ge(f_ready, s + 1)
                if not (isinstance(s, int) and s == 0):
                    pe.wait_ge(fused_ready, s)
                for a in range(P4):
                    for n, (w, f) in enumerate(((a_hi, f_hi), (a_hi, f_lo), (a_lo, f_hi))):
                        last = nc.tensor.matmul(fus[:, a, 0:HALF], w[:, par, :], f[:, a * HALF:(a + 1) * HALF],
                                                start=(n == 0), stop=(n == 2))
                last.then_inc(fuse_done, 1)

            def image(eng, b, par, first, last):
                def step(t, u, between={}):
                    s = b * T + t
                    convolve(t, par, u, s, between)
                    if not (first and isinstance(t, int) and t == 0):
                        fuse(s - 1, 1 - par if isinstance(t, int) and t == 0 else par)

                eng.wait_ge(w_ready, b + 1)
                step(0, 0)
                step(1, 1)
                with eng.Fori(1, T // 2 - 1) as j:
                    step(2 * j, 0)
                    step(2 * j + 1, 1)
                step(T - 2, 0, {} if last else {0: lambda: group_means(b + 1), 1: lambda: group_all(b + 1),
                                                14: lambda: generator(b + 1)})
                step(T - 1, 1)

            pe.wait_ge(const_load, 16)
            group_means(0)
            group_all(0)
            generator(0)
            images(pe, image)
            fuse(B * T - 1, (B - 1) % 2)


def layouts(x, w1, b1, w2, b2, lk, fw, fb):
    import numpy as np
    ix, iy, ci = np.meshgrid(np.arange(PW), np.arange(PH), np.arange(ATT), indexing="ij")
    ix, iy, ci = ix.ravel(), iy.ravel(), ci.ravel()
    ox, oyl, oyh, co = np.meshgrid(np.arange(PW), np.arange(2), np.arange(2), np.arange(ATT), indexing="ij")
    ox, oy, co = ox.ravel(), (2 * oyh + oyl).ravel(), co.ravel()
    wbase = np.zeros((128, NB, 128), lk.dtype)
    tap = np.zeros((128, NM, NPOS, NT), np.float32)
    for k, (by, bx) in enumerate(BLOCKS):
        ky = PH * by + iy[:, None] - oy[None, :]
        kx = PW * bx + ix[:, None] - ox[None, :]
        ok = (ky >= 0) & (ky < LK) & (kx >= 0) & (kx < LK)
        p, m = np.nonzero(ok)
        wbase[p, k, m] = lk[co[m], ci[p], ky[p, m], kx[p, m]]
        ty, tx = ky - (LK - SK) // 2, kx - (LK - SK) // 2
        ok = (ty >= 0) & (ty < SK) & (tx >= 0) & (tx < SK)
        if k < NM:
            p, m = np.nonzero(ok[:, ::ATT])
            tap[p, k, m, (SK * ty + tx)[:, ::ATT][p, m]] = 1.0
        else:
            assert not ok.any()
    kk = np.concatenate([np.repeat([0, 1], IDT), np.repeat([0, 1], ATT)])
    cc = np.concatenate([np.tile(np.arange(ATT, C), 2), np.tile(np.arange(ATT), 2)])
    f = np.zeros((128, 128), fw.dtype)
    same = kk[:, None] == kk[None, :]
    p, m = np.nonzero(same)
    f[p, m] = fw[cc[m], cc[p]]
    parts = {
        "gx": (cc[:, None] // 2 == cc[None, :] // 2) * np.float32(0.25),
        "ga": (cc[:, None] // 2 == ci[None, :] // 2) * np.float32(0.25),
        "ca": (cc[:, None] == ci[None, :]) * np.float32(0.5),
        "ones": np.full((128, 128), 1.0 / 8, np.float32),
        "fw": f,
        "w1": w1.T[ci],
        "b1": np.broadcast_to(b1, (128, HID)),
        "w2": w2.reshape(ATT, NT * HID)[ci],
        "b2": b2.reshape(ATT, NT)[ci],
        "fb": fb[cc][:, None],
        "delta": (ci[:, None] == np.arange(ATT)[None, :]) * np.float32(1),
        "rows": np.stack([cc < ATT, (cc >= ATT) / np.float32(ZS)], 1),
        "tap": tap.reshape(128, -1),
    }
    consts = np.zeros((128, NCONST), np.float32)
    for name, (a, n) in _C.items():
        consts[:, a:a + n] = parts[name]
    return wbase.reshape(128, NB * 128), consts


def kernel(**inputs):
    import numpy as np
    import concourse.bacc as bacc
    from concourse.bass_utils import run_bass_kernel_spmd

    v = {n.replace("L0_conv_", ""): np.ascontiguousarray(a) for n, a in inputs.items()}
    wbase, consts = layouts(v["x"], v["w1"], v["b1"], v["w2"], v["b2"], v["lk_filter"], v["fusion_w"], v["fusion_b"])
    arrays = {"in_x": v["x"], "in_wbase": wbase, "in_consts": consts}
    nc = bacc.Bacc("TRN2", target_bir_lowering=False, num_devices=1)
    args = [nc.dram_tensor(n, a.shape, mybir.dt.from_np(a.dtype), kind="ExternalInput").ap() for n, a in arrays.items()]
    out = nc.dram_tensor("out", (B, C, H, W), F32, kind="ExternalOutput").ap()
    build(nc, *args, out)
    r = run_bass_kernel_spmd(nc, [arrays], core_ids=[0])
    return r.results[0]["out"]
```

```python
from contextlib import ExitStack

import concourse.bass as bass
from concourse import mybir

F32 = mybir.dt.float32
F16 = mybir.dt.float16
ALU = mybir.AluOpType
ACT = mybir.ActivationFunctionType
AX = mybir.AxisListType

B, C, H, W = 16, 64, 192, 192
ATT = 16
IDT = C - ATT
HID = 8
LK, SK = 13, 3
PH, PW = 4, 2
NQ = H // PH
BY, BM = 4, 4
T = 12
TS = T // 2
P4 = NQ // T
P8 = 2 * P4
NW = W // 4
MW = NW + 1
PIX = P4 * 2 * W
HALF = 2 * W
R = 16
ZROWS = NQ + 1
ZS = 64.0
WS = 1024.0
WF = 24.0
TINY = 1e-30
MID = [(by, m) for by in (1, 2) for m in (0, 1)]
BLOCKS = MID + [(by, m) for by in range(BY) for m in range(-1, BM - 1) if (by, m) not in MID]
NM, NB = len(MID), len(BLOCKS)
NS = NB - NM
NPOS = PH * PW
NT = SK * SK
GN_EPS = 1e-5
EDGE = 6
CHAIN = 32
SCALES_AT = 11

_C = {}
_at = 0
for _name, _n in (("gx", 128), ("ga", 128), ("ca", 128), ("ones", 128), ("fw", 128), ("w1", HID), ("b1", HID),
                  ("w2", NT * HID), ("b2", NT), ("fb", 1), ("delta", ATT), ("rows", 2)):
    _C[_name] = (_at, _n)
    _at += _n
NCONST = _at


def build(nc, x, wbase, consts, tap, out):
    with ExitStack() as ctx:
        def sb(name, shape, dt=F32):
            return ctx.enter_context(nc.sbuf_tensor(name, shape, dt))

        def ps(name, shape):
            return ctx.enter_context(nc.psum_tensor(name, shape, F32))

        def sem(name):
            return ctx.enter_context(nc.semaphore(name))

        xr = sb("xr", [128, R, PIX])
        f_z = sb("f_z", [96, P4, HALF])
        f_hi = sb("f_hi", [128, 2, PIX], F16)
        f_lo = sb("f_lo", [128, 2, PIX], F16)
        raw = sb("raw", [128, 2, EDGE, W])
        z_f = sb("z_f", [128, EDGE, 4 * MW])
        z_sum = sb("z_sum", [128, EDGE, MW])
        z_hi = sb("z_hi", [128, 3, ZROWS, MW], F16)
        z_lo = sb("z_lo", [128, 3, ZROWS, MW], F16)
        m_base = sb("m_base", [128, 2, NM, 128])
        w_mid = sb("w_mid", [128, 2 * NM * NPOS, ATT])
        m_sum = sb("m_sum", [128, NM * NPOS * ATT])
        w_hi = sb("w_hi", [128, 3, NB, 128], F16)
        w_lo = sb("w_lo", [128, 3, NB, 128], F16)
        y_even = sb("y_even", [128, P8, NW])
        y_odd = sb("y_odd", [128, P8, NW])
        a_hi = sb("a_hi", [128, 2, 128], F16)
        a_lo = sb("a_lo", [128, 2, 128], F16)
        cst = sb("cst", [128, NCONST])
        taps = sb("taps", [128, 2 * NM * NPOS, NT], F16)
        s_base = xr[:, R - 2:R, :]
        s_sum = xr[:, R - 3:R - 2, :]
        stats = sb("stats", [128, T * 3, 6])
        st = sb("st", [128, 4])
        vg = sb("vg", [128, 2])
        root = sb("root", [128, 2])
        rstd = sb("rstd", [128, 2])
        newt = sb("newt", [128, 2])
        scl = sb("scl", [128, 2, 2])
        shf = sb("shf", [128, 2, 2])
        pooled = sb("pooled", [128, 1])
        pw1 = sb("pw1", [128, HID])
        hpre = sb("hpre", [128, HID])
        hid = sb("hid", [128, HID])
        kprod = sb("kprod", [128, NT, HID])
        kern = sb("kern", [128, NT])
        kmax = sb("kmax", [128, 1])
        wmax = sb("wmax", [128, 1])
        wsafe = sb("wsafe", [128, 1])
        wcap = sb("wcap", [128, 1])
        wscale = sb("wscale", [128, 1])
        abs1 = sb("abs1", [128, HID])
        absb = sb("absb", [128, HID])
        abs2 = sb("abs2", [128, NT * HID])
        absb2 = sb("absb2", [128, NT])
        mags = sb("mags", [128, 5])
        magmax = sb("magmax", [128, 5])
        lkmax = sb("lkmax", [128, 1])
        cscale = sb("cscale", [128, 2])
        vprod = sb("vprod", [128, 2 * NM * NPOS, NT])
        vtap = sb("vtap", [128, 2 * NM * NPOS])
        frow = sb("frow", [128, 1])
        avec = sb("avec", [128, 1])
        fscale = sb("fscale", [128, 2])
        unscale = sb("unscale", [128, 2])

        conv = ps("conv", [128, 3, 512])
        fus = ps("fus", [128, P4, 512])
        small = ps("small", [128, 512])

        x_first = [sem(f"x_first{k}") for k in range(4)]
        x_load = [sem(f"x_load{k}") for k in range(2)]
        x_store = sem("x_store")
        att_load = [sem(f"att_load{k}") for k in range(2)]
        const_load = sem("const_load")
        base_load = sem("base_load")
        zeroed = sem("zeroed")
        setup_chain = sem("setup_chain")
        bound_sum = sem("bound_sum")
        setup_max = sem("setup_max")
        same_high = sem("same_high")
        same_ready = sem("same_ready")
        conv_done = [sem(f"conv_done{k}") for k in range(3)]
        fuse_done = sem("fuse_done")
        fused_ready = sem("fused_ready")
        out_ready = sem("out_ready")
        f_norm = sem("f_norm")
        f_cast = sem("f_cast")
        f_split = sem("f_split")
        f_conv = sem("f_conv")
        f_ready = sem("f_ready")
        a_moved = sem("a_moved")
        b_copied = sem("b_copied")
        ab_ready = sem("ab_ready")
        even_ready = sem("even_ready")
        odd_ready = sem("odd_ready")
        z_norm = sem("z_norm")
        z_added = sem("z_added")
        z_high = sem("z_high")
        z_ready = sem("z_ready")
        stat_done = sem("stat_done")
        prep_dve = sem("prep_dve")
        group_mean = sem("group_mean")
        group_stats = sem("group_stats")
        hidden_pre = sem("hidden_pre")
        root_ready = sem("root_ready")
        hid_ready = sem("hid_ready")
        max_ready = sem("max_ready")
        mid_made = sem("mid_made")
        mid_high = sem("mid_high")
        mid_ready = sem("mid_ready")
        a_high = sem("a_high")
        a_ready = sem("a_ready")
        apart = sem("apart")

        block = ctx.enter_context(nc.Block())

        def c(name):
            a, n = _C[name]
            return cst[:, a:a + n]

        def mid(e):
            n = NM * NPOS
            return m_sum[:, :] if e == 2 else w_mid[:, e * n:(e + 1) * n, :].rearrange("p n m -> p (n m)")

        def same(e):
            return (s_sum if e == 2 else s_base[:, e:e + 1, :]).rearrange("p s n -> p (s n)")

        def place(f, j, e):
            on, oyl = j // 2, j % 2
            return f[96:128, :].rearrange("p (a l n o) -> p a l n o", a=P4, l=2, o=4)[:, :, oyl, :, 2 * on + e]

        x_v = x.rearrange("b c (p k l) w -> b k c p (l w)", k=2, l=2)
        out_v = out.rearrange("b c (p k l) w -> b k c p (l w)", k=2, l=2)
        att_v = x.rearrange("b c (p k l) w -> b k l c p w", k=2, l=2)

        def images(eng, image):
            image(eng, 0, 0, True, False)
            with eng.Fori(0, (B - 2) // 2) as i:
                image(eng, 2 * i + 1, 1, False, False)
                image(eng, 2 * i + 2, 0, False, False)
            image(eng, B - 1, (B - 1) % 2, False, True)

        def wait_apart(eng, waited, count):
            eng.wait_ge(waited, count)
            eng.sem_inc(apart, 1)

        def parts_of_x():
            for k in range(2):
                yield k, slice(48 * k, 48 * k + 48), slice(ATT, C)
                yield k, slice(96 + 16 * k, 112 + 16 * k), slice(0, ATT)

        @block.sync
        def _(sp):
            def load_x(b, t, slot, landed, before=None):
                if before is not None:
                    wait_apart(sp, landed, before)
                for k, part, ch in parts_of_x():
                    sp.dma_start(xr[part, bass.ds(slot, 1), :].rearrange("c s (p n) -> c (s p) n", p=P4),
                                 x_v[bass.ds(b, 1), k, ch, bass.ds(P4 * t, P4), :].rearrange("b c p n -> (b c) p n")
                                 ).then_inc(landed, 16)

            def store(b, t, slot, m):
                wait_apart(sp, out_ready, m + 1)
                for k, part, ch in parts_of_x():
                    sp.dma_start(out_v[bass.ds(b, 1), k, ch, bass.ds(P4 * t, P4), :].rearrange("b c p n -> (b c) p n"),
                                 xr[part, bass.ds(slot, 1), :].rearrange("c s (p n) -> c (s p) n", p=P4)
                                 ).then_inc(x_store, 16)
                wait_apart(sp, x_store, 64 * (m + 1))

            base_v = wbase.rearrange("p (e k) -> p e k", e=2)
            sp.dma_start(m_base[:, :, :, :].rearrange("p e k m -> p e (k m)"), base_v[:, :, 0:NM * 128]).then_inc(base_load, 16)
            sp.dma_start(s_base, base_v[:, :, NM * 128:]).then_inc(base_load, 16)
            for m in range(T):
                load_x(0, m, m, x_first[m % 4], 64 * (m // 4) if m >= 4 else None)
            for k in range(R - T):
                if k == 1:
                    sp.wait_ge(same_ready, 3)
                load_x(1, k, T + k, x_load[k % 2], 64 * (k // 2) if k >= 2 else None)
            with sp.Fori(0, B - 2) as b:
                with sp.Fori(0, 4) as g:
                    for u in range(2):
                        m = b * T + g * 2 + u
                        store(b, g * 2 + u, m % R, m)
                        load_x(b + 1, g * 2 + u + 4, m % R, x_load[u], 64 * (6 * b + g + 2))
                with sp.Fori(0, 2) as g:
                    for u in range(2):
                        m = b * T + 8 + g * 2 + u
                        store(b, 8 + g * 2 + u, m % R, m)
                        load_x(b + 2, g * 2 + u, m % R, x_load[u], 64 * (6 * b + g + 6))
            b = B - 2
            for t in range(8):
                store(b, t, (b * T + t) % R, b * T + t)
                load_x(b + 1, t + 4, (b * T + t) % R, x_load[t % 2], 64 * (6 * b + t // 2 + 2))
            for t in range(8, T):
                store(b, t, (b * T + t) % R, b * T + t)
            with sp.Fori(0, T) as t:
                m = (B - 1) * T + t
                store(B - 1, t, m % R, m)
            sp.wait_ge(x_store, 64 * B * T)

        def z_parts(t):
            both = [(0, 64), (64, 128)]
            if isinstance(t, int) and t == 0:
                return [(0, 1, 0, [(32, 64), (96, 128)]), (1, 5, 1, both)]
            if isinstance(t, int) and t == T - 1:
                return [(46, 2, 0, both), (48, 1, 2, [(0, 32), (64, 96)])]
            return [(P4 * t + 2, P4, 0, both)]

        def z_wide_parts(t):
            return [(q0, n, r0, [(0, 128)] if parts[0] == (0, 64) else parts) for q0, n, r0, parts in z_parts(t)]

        SETUP = 14

        @block.gpsimd
        def _(pool):
            def load_att(b, t, par, s):
                if s is not None:
                    pool.wait_ge(z_norm, s - 1)
                for ix in range(PW):
                    for h in range(2):
                        if isinstance(t, int) and t == 0:
                            p0, n, r0 = 0, 5 + h, 1 - h
                        elif isinstance(t, int) and t == T - 1:
                            p0, n, r0 = 45 + h, 3 - h, 0
                        else:
                            p0, n, r0 = P4 * t + 1 + h, P4, 0
                        at = 64 * ix + 32 * h
                        for l in range(2):
                            pool.dma_start(raw[at + 16 * l:at + 16 * l + 16, par, r0:r0 + n, :],
                                           att_v[bass.ds(b, 1), 1 - h, l, 0:ATT, bass.ds(p0, n), :]
                                           .rearrange("b c p w -> (b c) p w")).then_inc(att_load[par], 16)

            load_att(0, 0, 0, None)
            load_att(0, 1, 1, None)
            pool.wait_ge(setup_chain, SETUP)
            nc.gpsimd.partition_all_reduce(magmax[:, :], mags[:, :], 128, bass.bass_isa.ReduceOp.max).then_inc(setup_max, 1)

            def largest(b):
                wait_apart(pool, prep_dve, CHAIN * b + 19)
                nc.gpsimd.partition_all_reduce(wmax[:, :], kmax[:, :], 128,
                                               bass.bass_isa.ReduceOp.max).then_inc(max_ready, 1)

            def middle_blocks(b):
                wait_apart(pool, prep_dve, CHAIN * b + 21)
                nc.gpsimd.tensor_tensor(w_mid[:, :, :],
                                        vtap[:, :].rearrange("p (n o) -> p n o", o=1).to_broadcast([128, 2 * NM * NPOS, ATT]),
                                        c("delta").rearrange("p (o m) -> p o m", o=1).to_broadcast([128, 2 * NM * NPOS, ATT]),
                                        ALU.mult).then_inc(mid_made, 1)
                pool.wait_ge(mid_made, 3 * b + 1)
                nc.gpsimd.tensor_tensor(w_mid[:, :, :], w_mid[:, :, :],
                                        m_base[:, :, :, :].rearrange("p e k (n m) -> p (e k n) m", m=ATT),
                                        ALU.add).then_inc(mid_made, 1)
                pool.wait_ge(mid_made, 3 * b + 2)
                nc.gpsimd.tensor_tensor(m_sum[:, :], mid(0), mid(1), ALU.add).then_inc(mid_made, 1)

            def image(eng, b, par, first, last):
                load_att(b, 3, 1, b * T + 3)
                with eng.Fori(2, T // 2 - 1) as j:
                    for u in range(2):
                        load_att(b, 2 * j + u, u, b * T + 2 * j + u)
                for t in (T - 2, T - 1):
                    load_att(b, t, t % 2, b * T + t)
                if not last:
                    for t in range(3):
                        load_att(b + 1, t, t % 2, (b + 1) * T + t)
                    largest(b + 1)
                    middle_blocks(b + 1)

            load_att(0, 2, 0, 2)
            largest(0)
            middle_blocks(0)
            images(pool, image)

        @block.scalar
        def _(act):
            act.dma_start(cst[:, :], consts).then_inc(const_load, 16)
            act.dma_start(taps[:, :, :], tap.rearrange("p (n t) -> p n t", t=NT)).then_inc(const_load, 16)

            def evacuate(g, par):
                act.wait_ge(fuse_done, g + 1)
                nc.scalar.activation(fus[:, :, 0:HALF], fus[:, :, 0:HALF], ACT.Identity,
                                     bias=c("fb"), scale=unscale[:, par:par + 1]).then_inc(fused_ready, 1)

            def identity_part(g, par):
                for h in range(P4):
                    if not (isinstance(g, int) and g == 0):
                        act.wait_ge(f_split, P4 * g + h - 3)
                    src = xr[0:96, bass.ds(g % R, 1), h * HALF:(h + 1) * HALF].rearrange("p s n -> p (s n)")
                    nc.scalar.activation(f_z[:, h, :], src, ACT.Identity,
                                         bias=shf[0:96, par, 0:1], scale=scl[0:96, par, 0:1]).then_inc(f_norm, 1)

            def conv_part(g, h, s, e):
                act.wait_ge((even_ready, odd_ready)[e], s + 1)
                if h == 0 and e == 0 and not (isinstance(g, int) and g == 0):
                    act.wait_ge(fuse_done, g - 1)
                y = (y_even, y_odd)[e]
                for j in range(4):
                    last = nc.scalar.activation(place(f_hi[:, h, :], j, e), y[32 * j:32 * j + 32, P4 * h:P4 * h + P4, :], ACT.Copy)
                last.then_inc(f_conv, 1)

            def move_a(s, par):
                act.wait_ge(conv_done[0], s + 1)
                if not (isinstance(s, int) and s == 0):
                    act.wait_ge(f_ready, 2 * s)
                a = conv[:, 0, 0:P8 * MW].rearrange("p (a n) -> p a n", a=P8)
                nc.scalar.activation(y_odd[0:64, :, :], a[64:128, :, 0:NW], ACT.Copy, scale=cscale[64:128, par:par + 1])
                nc.scalar.activation(y_odd[64:128, :, :], a[0:64, :, 1:MW], ACT.Copy,
                                     scale=cscale[0:64, par:par + 1]).then_inc(a_moved, 1)

            def copy_b(s, par):
                act.wait_ge(conv_done[1], s + 1)
                nc.scalar.activation(y_even[:, :, :], conv[:, 1, 0:P8 * NW].rearrange("p (a n) -> p a n", a=P8), ACT.Copy,
                                     scale=cscale[:, par:par + 1]).then_inc(b_copied, 1)

            def z_piece(t, par, ipar, s):
                act.wait_ge(att_load[par], 128 * ((s - par) // 2 + 1) if isinstance(s, int) else (s - par) * 64 + 128)
                if not (isinstance(s, int) and s == 0):
                    act.wait_ge(z_ready, s)
                for q0, n, r0, parts in z_parts(t):
                    for a, b in parts:
                        j0 = 2 if a < 64 else 0
                        last = nc.scalar.activation(z_f[a:b, r0:r0 + n, j0:j0 + W], raw[a:b, par, r0:r0 + n, :], ACT.Identity,
                                                    bias=shf[a:b, ipar, 1:2], scale=scl[a:b, ipar, 1:2])
                last.then_inc(z_norm, 1)
                act.wait_ge(z_norm, s + 1)
                for q0, n, r0, parts in z_wide_parts(t):
                    for a, b in parts:
                        for e in range(2):
                            nc.scalar.activation(z_hi[a:b, e, bass.ds(q0, n), :], z_f[a:b, r0:r0 + n, e:4 * MW:4], ACT.Copy)
                act.wait_ge(z_added, s + 1)
                for q0, n, r0, parts in z_wide_parts(t):
                    for a, b in parts:
                        last = nc.scalar.activation(z_hi[a:b, 2, bass.ds(q0, n), :], z_sum[a:b, r0:r0 + n, :], ACT.Copy)
                last.then_inc(z_high, 1)

            def prep_root(b):
                act.wait_ge(prep_dve, CHAIN * b + 4)
                nc.scalar.activation(root[:, :], vg[:, :], ACT.Sqrt).then_inc(root_ready, 1)

            def prep_hidden(b):
                act.wait_ge(prep_dve, CHAIN * b + 14)
                nc.scalar.activation(hid[:, :], hpre[:, :], ACT.Gelu).then_inc(hid_ready, 1)

            def high_of(b, e, s):
                act.wait_ge(mid_made, 3 * b + (3 if e == 2 else 2))
                if s is not None:
                    act.wait_ge(conv_done[e], s)
                nc.scalar.activation(w_hi[:, e, 0:NM, :].rearrange("p k m -> p (k m)"), mid(e), ACT.Copy,
                                     scale=wscale[:, 0:1]).then_inc(mid_high, 1)

            def high_of_fusion(b, par):
                act.wait_ge(prep_dve, CHAIN * b + CHAIN)
                nc.scalar.activation(a_hi[:, par, :], c("fw"), ACT.Copy, scale=avec[:, 0:1]).then_inc(a_high, 1)

            def image(eng, b, par, first, last):
                def step(t):
                    s = b * TS + t
                    at = t if isinstance(t, int) else None
                    old = 1 - par if at == 0 else par
                    begin = first and at == 0
                    ahead = at == TS - 1 and not last
                    if not begin:
                        conv_part(2 * s - 2, 0, s - 1, 1)
                        conv_part(2 * s - 1, 1, s - 1, 0)
                        conv_part(2 * s - 1, 1, s - 1, 1)
                    if at == 0 and not first:
                        for e in range(3):
                            high_of(b, e, s)
                        evacuate(2 * s - 2, old)
                    if at != TS - 1:
                        z_piece(2 * t + 2, 0, par, 2 * s + 2)
                    if at != 0:
                        evacuate(2 * s - 2, old)
                    identity_part(2 * s, par)
                    if ahead:
                        prep_root(b + 1)
                    if at != 0:
                        move_a(s, par)
                    if at != TS - 1:
                        z_piece(2 * t + 3, 1, par, 2 * s + 3)
                    elif not last:
                        act.wait_ge(prep_dve, CHAIN * (b + 1) + SCALES_AT)
                        z_piece(0, 0, 1 - par, 2 * s + 2)
                        copy_b(s, par)
                        z_piece(1, 1, 1 - par, 2 * s + 3)
                        prep_hidden(b + 1)
                        evacuate(2 * s - 1, par)
                    if at == 0:
                        if not first:
                            high_of_fusion(b, par)
                        move_a(s, par)
                        copy_b(s, par)
                        if not first:
                            evacuate(2 * s - 1, old)
                    identity_part(2 * s + 1, par)
                    if at != 0 and not ahead:
                        evacuate(2 * s - 1, old)
                        copy_b(s, par)
                    conv_part(2 * s, 0, s, 0)

                step(0)
                with eng.Fori(1, TS - 2) as t:
                    step(t)
                step(TS - 2)
                step(TS - 1)

            for e in range(3):
                act.wait_ge(setup_chain, SETUP + (7 if e == 2 else 6))
                nc.scalar.activation(w_hi[:, e, NM:NB, :].rearrange("p k m -> p (k m)"), same(e), ACT.Copy,
                                     scale=wscale[:, 0:1]).then_inc(same_high, 1)
            act.wait_ge(zeroed, 9)
            prep_root(0)
            act.wait_ge(prep_dve, SCALES_AT)
            for k in range(2):
                z_piece(k, k, 0, k)
            prep_hidden(0)
            for e in range(3):
                high_of(0, e, None)
            high_of_fusion(0, 0)
            images(act, image)
            steps, lpar = B * TS, (B - 1) % 2
            conv_part(2 * steps - 2, 0, steps - 1, 1)
            conv_part(2 * steps - 1, 1, steps - 1, 0)
            conv_part(2 * steps - 1, 1, steps - 1, 1)
            evacuate(2 * steps - 2, lpar)
            evacuate(2 * steps - 1, lpar)

        @block.vector
        def _(dve):
            def residual(g):
                dve.wait_ge(fused_ready, g + 1)
                dst = xr[:, bass.ds(g % R, 1), :].rearrange("p s (a n) -> p (s a) n", a=P4)
                nc.vector.tensor_tensor(dst, dst, fus[:, :, 0:HALF], ALU.add).then_inc(out_ready, 1)

            def identity_split(g, k):
                if not (isinstance(g, int) and g < 2):
                    dve.wait_ge(fuse_done, g - 1)
                for h in range(P4 + 1):
                    if h < P4:
                        dve.wait_ge(f_norm, P4 * g + h + 1)
                        nc.vector.tensor_copy(f_hi[0:96, k, h * HALF:(h + 1) * HALF], f_z[:, h, :]).then_inc(f_cast, 1)
                    if h > 0:
                        at = slice((h - 1) * HALF, h * HALF)
                        dve.wait_ge(f_cast, P4 * g + h)
                        nc.vector.tensor_tensor(f_lo[0:96, k, at], f_z[:, h - 1, :], f_hi[0:96, k, at],
                                                ALU.subtract).then_inc(f_split, 1)

            def conv_low(g, h, e):
                dve.wait_ge(f_conv, 2 * g + e + 1)
                y = (y_even, y_odd)[e]
                for j in range(4):
                    last = nc.vector.tensor_tensor(place(f_lo[:, h, :], j, e), y[32 * j:32 * j + 32, P4 * h:P4 * h + P4, :],
                                                   place(f_hi[:, h, :], j, e), ALU.subtract)
                if e == 1:
                    last.then_inc(f_ready, 1)

            def even_columns(s, par):
                dve.wait_ge(a_moved, s + 1)
                dve.wait_ge(b_copied, s + 1)
                nc.vector.tensor_tensor(y_odd[:, :, :], y_odd[:, :, :], y_even[:, :, :], ALU.add).then_inc(ab_ready, 1)
                dve.wait_ge(ab_ready, s + 1)
                a = conv[:, 0, 0:P8 * MW].rearrange("p (a n) -> p a n", a=P8)[:, :, 0:NW]
                nc.vector.scalar_tensor_tensor(out=y_even[:, :, :], in0=a, scalar=cscale[:, par:par + 1], in1=y_even[:, :, :],
                                               op0=ALU.mult, op1=ALU.add).then_inc(even_ready, 1)

            def odd_columns(s, par):
                dve.wait_ge(conv_done[2], s + 1)
                dve.wait_ge(even_ready, s + 1)
                nc.vector.scalar_tensor_tensor(out=y_odd[:, :, :], in0=conv[:, 2, 0:P8 * NW].rearrange("p (a n) -> p a n", a=P8),
                                               scalar=cscale[:, par:par + 1], in1=y_odd[:, :, :],
                                               op0=ALU.mult, op1=ALU.subtract).then_inc(odd_ready, 1)

            def z_split(t, s):
                dve.wait_ge(z_norm, s + 1)
                for q0, n, r0, parts in z_wide_parts(t):
                    for a, b in parts:
                        last = nc.vector.tensor_tensor(z_sum[a:b, r0:r0 + n, :], z_f[a:b, r0:r0 + n, 1:4 * MW:4],
                                                       z_f[a:b, r0:r0 + n, 2:4 * MW:4], ALU.add)
                last.then_inc(z_added, 1)
                dve.wait_ge(z_high, s + 1)
                dve.wait_ge(z_added, s + 1)
                for q0, n, r0, parts in z_wide_parts(t):
                    for a, b in parts:
                        rows = bass.ds(q0, n)
                        for e in range(2):
                            nc.vector.tensor_tensor(z_lo[a:b, e, rows, :], z_f[a:b, r0:r0 + n, e:4 * MW:4],
                                                    z_hi[a:b, e, rows, :], ALU.subtract)
                        last = nc.vector.tensor_tensor(z_lo[a:b, 2, rows, :], z_sum[a:b, r0:r0 + n, :],
                                                       z_hi[a:b, 2, rows, :], ALU.subtract)
                last.then_inc(z_ready, 1)

            def statistics(t, m, landed, count):
                dve.wait_ge(landed, count)
                for n in range(3):
                    nc.vector.bn_stats(stats[:, bass.ds(3 * t + n, 1), :].rearrange("p s n -> p (s n)"),
                                       xr[:, bass.ds(m % R, 1), 512 * n:512 * n + 512].rearrange("p s n -> p (s n)")
                                       ).then_inc(stat_done, 1)

            linked = [0]

            def link_of(b, first):
                linked[0] = first

                def link(ins):
                    ins.then_inc(prep_dve, 1)
                    linked[0] += 1
                    dve.wait_ge(prep_dve, CHAIN * b + linked[0])

                return link

            def prepare_mean(b):
                link = link_of(b, 0)
                wait_apart(dve, stat_done, 3 * T * b + 3 * T)
                link(nc.vector.bn_aggr(st[:, 0:2], stats[:, :, :].rearrange("p s n -> p (s n)")))

            def prepare_deviation(b):
                link = link_of(b, 1)
                dve.wait_ge(group_mean, b + 1)
                link(nc.vector.tensor_tensor(st[:, 2:3], st[:, 0:1], small[:, 0:1], ALU.subtract))
                link(nc.vector.scalar_tensor_tensor(out=st[:, 3:4], in0=st[:, 2:3], scalar=st[:, 2:3], in1=st[:, 1:2],
                                                    op0=ALU.mult, op1=ALU.add))

            def prepare_variance(b):
                link = link_of(b, 3)
                dve.wait_ge(group_stats, b + 1)
                link(nc.vector.tensor_scalar(vg[:, :], small[:, 7:12:4], GN_EPS, None, ALU.add))

            def prepare_scales(b, par):
                link = link_of(b, 4)
                dve.wait_ge(root_ready, b + 1)
                link(nc.vector.reciprocal(rstd[:, :], root[:, :]))
                link(nc.vector.tensor_tensor(newt[:, :], rstd[:, :], rstd[:, :], ALU.mult))
                link(nc.vector.tensor_tensor(newt[:, :], newt[:, :], vg[:, :], ALU.mult))
                link(nc.vector.tensor_scalar(newt[:, :], newt[:, :], -0.5, 1.5, ALU.mult, ALU.add))
                link(nc.vector.tensor_tensor(rstd[:, :], rstd[:, :], newt[:, :], ALU.mult))
                link(nc.vector.tensor_scalar(scl[:, par, :], rstd[:, :], ZS, None, ALU.mult))
                link(nc.vector.scalar_tensor_tensor(out=shf[:, par, :], in0=small[:, 4:9:4], scalar=-1.0, in1=scl[:, par, :],
                                                    op0=ALU.mult, op1=ALU.mult))
                link(nc.vector.tensor_tensor(pooled[:, :], small[:, 14:15], rstd[:, 1:2], ALU.mult))
                link(nc.vector.tensor_scalar(pw1[:, :], c("w1"), pooled[:, 0:1], None, ALU.mult))

            def prepare_kernel(b):
                link = link_of(b, 13)
                dve.wait_ge(hidden_pre, b + 1)
                link(nc.vector.tensor_tensor(hpre[:, :], small[:, 16:16 + HID], c("b1"), ALU.add))
                dve.wait_ge(hid_ready, b + 1)
                link(nc.vector.tensor_tensor(kprod[:, :, :], c("w2").rearrange("p (t j) -> p t j", j=HID),
                                             hid[:, :].rearrange("p (o j) -> p o j", o=1).to_broadcast([128, NT, HID]), ALU.mult))
                link(nc.vector.tensor_reduce(kern[:, :], kprod[:, :, :], AX.X, ALU.add))
                link(nc.vector.tensor_tensor(kern[:, :], kern[:, :], c("b2"), ALU.add))
                link(nc.vector.tensor_reduce(kmax[:, :], kern[:, :], AX.X, ALU.max, apply_absolute_value=True))
                link(nc.vector.tensor_tensor(kmax[:, :], kmax[:, :], lkmax[:, :], ALU.max))
                link(nc.vector.tensor_tensor(vprod[:, :, :], taps[:, :, :],
                                             kern[:, :].rearrange("p (o t) -> p o t", o=1).to_broadcast([128, 2 * NM * NPOS, NT]),
                                             ALU.mult))
                link(nc.vector.tensor_reduce(vtap[:, :], vprod[:, :, :], AX.X, ALU.add))

            def prepare_results(b, par):
                link = link_of(b, 21)
                dve.wait_ge(max_ready, b + 1)
                link(nc.vector.tensor_scalar(wsafe[:, :], wmax[:, :], TINY, None, ALU.max))
                link(nc.vector.tensor_scalar(avec[:, :], wsafe[:, :], c("rows")[:, 0:1], c("rows")[:, 1:2], ALU.mult, ALU.add))
                link(nc.vector.scalar_tensor_tensor(out=fscale[:, 0:1], in0=wsafe[:, :], scalar=magmax[:, 1:2], in1=magmax[:, 0:1],
                                                    op0=ALU.mult, op1=ALU.max))
                link(nc.vector.tensor_scalar(fscale[:, 0:1], fscale[:, 0:1], TINY, None, ALU.max))
                link(nc.vector.reciprocal(fscale[:, 1:2], fscale[:, 0:1]))
                link(nc.vector.tensor_scalar(fscale[:, 1:2], fscale[:, 1:2], WS, None, ALU.mult))
                link(nc.vector.tensor_tensor(avec[:, :], avec[:, :], fscale[:, 1:2], ALU.mult))
                link(nc.vector.tensor_scalar(unscale[:, par:par + 1], fscale[:, 0:1], 1.0 / WS, None, ALU.mult))
                link(nc.vector.tensor_tensor(wsafe[:, :], wsafe[:, :], wscale[:, :], ALU.mult))
                link(nc.vector.reciprocal(wsafe[:, :], wsafe[:, :]))
                link(nc.vector.tensor_scalar(cscale[:, par:par + 1], wsafe[:, :], 1.0 / ZS, None, ALU.mult))

            def low_of(b, e):
                dve.wait_ge(mid_high, 3 * b + e + 1)
                nc.vector.scalar_tensor_tensor(out=w_lo[:, e, 0:NM, :].rearrange("p k m -> p (k m)"),
                                               in0=mid(e), scalar=wscale[:, 0:1],
                                               in1=w_hi[:, e, 0:NM, :].rearrange("p k m -> p (k m)"),
                                               op0=ALU.mult, op1=ALU.subtract).then_inc(mid_ready, 1)

            def low_of_fusion(b, par):
                dve.wait_ge(a_high, b + 1)
                nc.vector.scalar_tensor_tensor(out=a_lo[:, par, :], in0=c("fw"), scalar=avec[:, 0:1], in1=a_hi[:, par, :],
                                               op0=ALU.mult, op1=ALU.subtract).then_inc(a_ready, 1)

            def image(eng, b, par, first, last):
                def stat(t, odd):
                    count = 64 * (6 * b + (t - odd) // 2 + 1) if isinstance(t, int) else 64 * (6 * b + 1) + 32 * (t - odd)
                    statistics(t, (b + 1) * T + t, x_load[odd], count)

                def step(t):
                    s = b * TS + t
                    at = t if isinstance(t, int) else None
                    begin = first and at == 0
                    ahead = at == TS - 1 and not last
                    if not begin:
                        conv_low(2 * s - 2, 0, 1)
                    if ahead:
                        identity_split(2 * s - 1, 1)
                        stat(T - 1, 1)
                        prepare_mean(b + 1)
                        conv_low(2 * s - 1, 1, 0)
                        conv_low(2 * s - 1, 1, 1)
                        prepare_deviation(b + 1)
                        residual(2 * s - 2)
                        prepare_variance(b + 1)
                        prepare_scales(b + 1, 1 - par)
                        identity_split(2 * s, 0)
                        z_split(0, 2 * s + 2)
                        even_columns(s, par)
                        z_split(1, 2 * s + 3)
                        prepare_kernel(b + 1)
                        residual(2 * s - 1)
                    else:
                        if not begin:
                            identity_split(2 * s - 1, 1)
                            conv_low(2 * s - 1, 1, 0)
                            conv_low(2 * s - 1, 1, 1)
                        if at == 0 and not first:
                            residual(2 * s - 2)
                            z_split(2, 2 * s + 2)
                            for e in range(3):
                                low_of(b, e)
                            prepare_results(b, par)
                        elif at != TS - 1:
                            z_split(2 * t + 2, 2 * s + 2)
                        if at != 0:
                            residual(2 * s - 2)
                            if not last:
                                stat(2 * t - 1, 1)
                        if at == 0:
                            z_split(3, 2 * s + 3)
                        identity_split(2 * s, 0)
                        if at == 0:
                            even_columns(s, par)
                            if not first:
                                low_of_fusion(b, par)
                                residual(2 * s - 1)
                        elif at != TS - 1:
                            z_split(2 * t + 3, 2 * s + 3)
                        if not last:
                            stat(2 * t, 0)
                        if at != 0:
                            residual(2 * s - 1)
                            even_columns(s, par)
                        if at == TS - 2 and not last:
                            stat(T - 3, 1)
                            stat(T - 2, 0)
                    conv_low(2 * s, 0, 0)
                    odd_columns(s, par)

                step(0)
                with eng.Fori(1, TS - 2) as t:
                    step(t)
                step(TS - 2)
                step(TS - 1)

            nc.vector.memset(z_f[:, :, :], 0.0).then_inc(zeroed, 1)
            for q, h in ((0, 0), (ZROWS - 1, 1)):
                for ix in range(PW):
                    for z in (z_hi, z_lo):
                        at = 64 * ix + 32 * h
                        nc.vector.memset(z[at:at + 32, :, q, :], 0.0).then_inc(zeroed, 1)
            count = [0]

            def setup(ins):
                ins.then_inc(setup_chain, 1)
                count[0] += 1
                dve.wait_ge(setup_chain, count[0])

            def magnitude(out_, in_):
                setup(nc.vector.scalar_tensor_tensor(out=out_, in0=in_, scalar=-1.0, in1=in_, op0=ALU.mult, op1=ALU.max))

            dve.wait_ge(const_load, 32)
            magnitude(abs1[:, :], c("w1"))
            magnitude(absb[:, :], c("b1"))
            magnitude(abs2[:, :], c("w2"))
            magnitude(absb2[:, :], c("b2"))
            setup(nc.vector.tensor_reduce(frow[:, :], c("fw"), AX.X, ALU.max, apply_absolute_value=True))
            setup(nc.vector.tensor_tensor(mags[:, 0:1], frow[:, :], c("rows")[:, 1:2], ALU.mult))
            setup(nc.vector.tensor_tensor(mags[:, 1:2], frow[:, :], c("rows")[:, 0:1], ALU.mult))
            dve.wait_ge(bound_sum, 1)
            setup(nc.vector.tensor_tensor(hpre[:, :], absb[:, :], small[:, 16:16 + HID], ALU.add))
            setup(nc.vector.tensor_tensor(kprod[:, :, :], abs2[:, :].rearrange("p (t j) -> p t j", j=HID),
                                          hpre[:, :].rearrange("p (o j) -> p o j", o=1).to_broadcast([128, NT, HID]), ALU.mult))
            setup(nc.vector.tensor_reduce(kern[:, :], kprod[:, :, :], AX.X, ALU.add))
            setup(nc.vector.tensor_tensor(kern[:, :], kern[:, :], absb2[:, :], ALU.add))
            setup(nc.vector.tensor_reduce(mags[:, 4:5], kern[:, :], AX.X, ALU.max))
            dve.wait_ge(base_load, 32)
            setup(nc.vector.tensor_reduce(mags[:, 2:3], m_base[:, :, :, :].rearrange("p e k m -> p (e k m)"), AX.X, ALU.max,
                                          apply_absolute_value=True))
            setup(nc.vector.tensor_reduce(mags[:, 3:4], s_base.rearrange("p e n -> p (e n)"), AX.X, ALU.max,
                                          apply_absolute_value=True))
            assert count[0] == SETUP
            dve.wait_ge(setup_max, 1)
            setup(nc.vector.tensor_tensor(lkmax[:, :], magmax[:, 2:3], magmax[:, 3:4], ALU.max))
            setup(nc.vector.tensor_scalar(wcap[:, :], lkmax[:, :], magmax[:, 4:5], 1.0 / WF, ALU.add, ALU.mult))
            setup(nc.vector.tensor_tensor(wcap[:, :], wcap[:, :], lkmax[:, :], ALU.max))
            setup(nc.vector.tensor_scalar(wcap[:, :], wcap[:, :], TINY, None, ALU.max))
            setup(nc.vector.reciprocal(wscale[:, :], wcap[:, :]))
            setup(nc.vector.tensor_scalar(wscale[:, :], wscale[:, :], WS, None, ALU.mult))
            setup(nc.vector.tensor_tensor(same(2), same(0), same(1), ALU.add))

            def low_of_same(e):
                dve.wait_ge(same_high, e + 1)
                nc.vector.scalar_tensor_tensor(out=w_lo[:, e, NM:NB, :].rearrange("p k m -> p (k m)"), in0=same(e),
                                               scalar=wscale[:, 0:1], in1=w_hi[:, e, NM:NB, :].rearrange("p k m -> p (k m)"),
                                               op0=ALU.mult, op1=ALU.subtract).then_inc(same_ready, 1)
            for t in range(T):
                statistics(t, t, x_first[t % 4], 64 * (t // 4 + 1))
            prepare_mean(0)
            prepare_deviation(0)
            low_of_same(0)
            prepare_variance(0)
            prepare_scales(0, 0)
            low_of_same(1)
            for k in range(2):
                z_split(k, k)
            low_of_same(2)
            prepare_kernel(0)
            for e in range(3):
                low_of(0, e)
            prepare_results(0, 0)
            low_of_fusion(0, 0)
            images(dve, image)
            steps = B * TS
            conv_low(2 * steps - 2, 0, 1)
            identity_split(2 * steps - 1, 1)
            conv_low(2 * steps - 1, 1, 0)
            conv_low(2 * steps - 1, 1, 1)
            residual(2 * steps - 2)
            residual(2 * steps - 1)

        @block.tensor
        def _(pe):
            def group_means(b):
                pe.wait_ge(prep_dve, CHAIN * b + 1)
                nc.tensor.matmul(small[:, 0:1], c("gx"), st[:, 0:1], start=True, stop=True).then_inc(group_mean, 1)

            def group_all(b):
                pe.wait_ge(prep_dve, CHAIN * b + 3)
                for n, m in enumerate(("gx", "ga", "ca")):
                    last = nc.tensor.matmul(small[:, 4 + 4 * n:8 + 4 * n], c(m), st[:, :], start=True, stop=True)
                last.then_inc(group_stats, 1)

            def generator(b):
                pe.wait_ge(prep_dve, CHAIN * b + 13)
                nc.tensor.matmul(small[:, 16:16 + HID], c("ones"), pw1[:, :], start=True, stop=True).then_inc(hidden_pre, 1)

            def convolve(e, t, between, start, end):
                at = t if isinstance(t, int) else None
                wide = MW if e == 0 else NW
                out = conv[:, e, 0:P8 * wide].rearrange("p (a n) -> p a n", a=P8)
                whole = (0, 0) if at == TS - 1 else (BY - 1, 0)
                order = [BLOCKS.index(whole)] + [k for k in range(NM, NB) if BLOCKS[k] != whole] + list(range(NM))
                for i in range(start, end):
                    k = order[i]
                    if i in between:
                        between[i]()
                    by, m = BLOCKS[k]
                    n0, n1 = max(0, -m), min(wide, MW - m)
                    a0 = 1 if by == 0 and at == 0 else 0
                    a1 = P8 - 1 if by == BY - 1 and at == TS - 1 else P8
                    rows = bass.ds(P8 * t + by - 1 + a0, a1 - a0)
                    for n, (w, z) in enumerate(((w_hi, z_hi), (w_hi, z_lo), (w_lo, z_hi))):
                        last = nc.tensor.matmul(out[:, a0:a1, n0:n1], w[:, e, k, :], z[:, e, rows, n0 + m:n1 + m],
                                                start=(i == 0 and n == 0), stop=(i == NB - 1 and n == 2))
                if end == NB:
                    last.then_inc(conv_done[e], 1)

            def fuse(g, k, par):
                pe.wait_ge(f_ready, g + 1)
                if not (isinstance(g, int) and g == 0):
                    pe.wait_ge(out_ready, g)
                for a in range(P4):
                    for n, (w, f) in enumerate(((a_hi, f_hi), (a_hi, f_lo), (a_lo, f_hi))):
                        last = nc.tensor.matmul(fus[:, a, 0:HALF], w[:, par, :], f[:, k, a * HALF:(a + 1) * HALF],
                                                start=(n == 0), stop=(n == 2))
                last.then_inc(fuse_done, 1)

            def image(eng, b, par, first, last):
                def step(t):
                    s = b * TS + t
                    at = t if isinstance(t, int) else None
                    old = 1 - par if at == 0 else par
                    begin = first and at == 0

                    def wait_for_a():
                        pe.wait_ge(z_ready, 2 * s + 2)
                        if begin:
                            pe.wait_ge(same_ready, 1)
                        else:
                            pe.wait_ge(even_ready, s)

                    def wait_for_b():
                        if begin:
                            pe.wait_ge(same_ready, 2)
                        else:
                            pe.wait_ge(b_copied, s)

                    def wait_for_c():
                        if begin:
                            pe.wait_ge(same_ready, 3)
                        else:
                            pe.wait_ge(odd_ready, s)

                    def middle(e):
                        wait_apart(pe, mid_ready, 3 * b + e + 1)
                        convolve(e, t, {}, NS, NB)

                    fuse_0, fuse_1 = [(lambda: None) if begin else (lambda k=k: fuse(2 * s - 2 + k, k, old)) for k in range(2)]
                    if at == 0:
                        wait_for_a()
                        convolve(0, t, {}, 0, NS)
                        wait_for_b()
                        convolve(1, t, {8: fuse_0}, 0, NS)
                        wait_for_c()
                        convolve(2, t, {6: fuse_1}, 0, 8)
                        middle(0)
                        middle(1)
                        convolve(2, t, {}, 8, NS)
                        middle(2)
                        wait_apart(pe, a_ready, b + 1)
                    else:
                        in_b, in_c = {13: fuse_1}, {}
                        if at == TS - 1 and not last:
                            in_b = {4: lambda: group_means(b + 1), 8: lambda: group_all(b + 1), 14: fuse_1}
                            in_c = {1: lambda: generator(b + 1)}
                        wait_for_a()
                        convolve(0, t, {14: fuse_0}, 0, NB)
                        wait_for_b()
                        convolve(1, t, in_b, 0, NB)
                        wait_for_c()
                        convolve(2, t, in_c, 0, NB)

                step(0)
                with eng.Fori(1, TS - 2) as t:
                    step(t)
                step(TS - 2)
                step(TS - 1)

            pe.wait_ge(setup_chain, 1)
            nc.tensor.matmul(small[:, 16:16 + HID], c("ones"), abs1[:, :], start=True, stop=True).then_inc(bound_sum, 1)
            group_means(0)
            group_all(0)
            generator(0)
            images(pe, image)
            fuse(B * T - 2, 0, (B - 1) % 2)
            fuse(B * T - 1, 1, (B - 1) % 2)


def layouts(x, w1, b1, w2, b2, lk, fw, fb):
    import numpy as np
    ix, iy, ci = np.meshgrid(np.arange(PW), np.arange(PH), np.arange(ATT), indexing="ij")
    ix, iy, ci = ix.ravel(), iy.ravel(), ci.ravel()
    ox, oyl, oyh, co = np.meshgrid(np.arange(PW), np.arange(2), np.arange(2), np.arange(ATT), indexing="ij")
    ox, oy, co = ox.ravel(), (2 * oyh + oyl).ravel(), co.ravel()
    wbase = np.zeros((128, 2, NB, 128), lk.dtype)
    tap = np.zeros((128, 2, NM, NPOS, NT), np.float16)
    for e in range(2):
        for k, (by, m) in enumerate(BLOCKS):
            ky = PH * by + iy[:, None] - oy[None, :]
            kx = 2 * (2 * m + ix[:, None] - ox[None, :] + 2) + e
            ok = (ky >= 0) & (ky < LK) & (kx >= 0) & (kx < LK)
            p, o = np.nonzero(ok)
            wbase[p, e, k, o] = lk[co[o], ci[p], ky[p, o], kx[p, o]]
            ty, tx = ky - (LK - SK) // 2, kx - (LK - SK) // 2
            ok = (ty >= 0) & (ty < SK) & (tx >= 0) & (tx < SK)
            if k < NM:
                p, o = np.nonzero(ok[:, ::ATT])
                tap[p, e, k, o, (SK * ty + tx)[:, ::ATT][p, o]] = 1.0
            else:
                assert not ok.any()
    kk = np.concatenate([np.repeat([0, 1], IDT), np.repeat([0, 1], ATT)])
    cc = np.concatenate([np.tile(np.arange(ATT, C), 2), np.tile(np.arange(ATT), 2)])
    f = np.zeros((128, 128), fw.dtype)
    same = kk[:, None] == kk[None, :]
    p, m = np.nonzero(same)
    f[p, m] = fw[cc[m], cc[p]]
    parts = {
        "gx": (cc[:, None] // 2 == cc[None, :] // 2) * np.float32(0.25),
        "ga": (cc[:, None] // 2 == ci[None, :] // 2) * np.float32(0.25),
        "ca": (cc[:, None] == ci[None, :]) * np.float32(0.5),
        "ones": np.full((128, 128), 1.0 / 8, np.float32),
        "fw": f,
        "w1": w1.T[ci],
        "b1": np.broadcast_to(b1, (128, HID)),
        "w2": w2.reshape(ATT, NT * HID)[ci],
        "b2": b2.reshape(ATT, NT)[ci],
        "fb": fb[cc][:, None],
        "delta": (ci[:, None] == np.arange(ATT)[None, :]) * np.float32(1),
        "rows": np.stack([cc < ATT, (cc >= ATT) / np.float32(ZS)], 1),
    }
    consts = np.zeros((128, NCONST), np.float32)
    for name, (a, n) in _C.items():
        consts[:, a:a + n] = parts[name]
    return wbase.reshape(128, 2 * NB * 128), consts, tap.reshape(128, -1)


def kernel(**inputs):
    import numpy as np
    import concourse.bacc as bacc
    from concourse.bass_utils import run_bass_kernel_spmd

    v = {n.replace("L0_conv_", ""): np.ascontiguousarray(a) for n, a in inputs.items()}
    wbase, consts, tap = layouts(v["x"], v["w1"], v["b1"], v["w2"], v["b2"], v["lk_filter"], v["fusion_w"], v["fusion_b"])
    arrays = {"in_x": v["x"], "in_wbase": wbase, "in_consts": consts, "in_tap": tap}
    nc = bacc.Bacc("TRN2", target_bir_lowering=False, num_devices=1)
    args = [nc.dram_tensor(n, a.shape, mybir.dt.from_np(a.dtype), kind="ExternalInput").ap() for n, a in arrays.items()]
    out = nc.dram_tensor("out", (B, C, H, W), F32, kind="ExternalOutput").ap()
    build(nc, *args, out)
    r = run_bass_kernel_spmd(nc, [arrays], core_ids=[0])
    return r.results[0]["out"]
```
